# Optimizing a Trainium2 kernel written in Bass

```python
import numpy as np
import jax
import jax.numpy as jnp

def _softmax(x, axis=-1):
    return jax.nn.softmax(x, axis=axis)

def _gelu(x):
    return jax.nn.gelu(x, approximate=True)

def _silu(x):
    return jax.nn.silu(x)

def _sigmoid(x):
    return jax.nn.sigmoid(x)

def _layernorm(x, axis=-1, eps=1e-05):
    m = jnp.mean(x, axis=axis, keepdims=True)
    v = jnp.var(x, axis=axis, keepdims=True)
    return (x - m) / jnp.sqrt(v + eps)

def _scatter_add(tgt, idx, src, axis=0):
    return tgt.at[idx].add(src)

def _segment_sum(src, seg, n):
    return jax.ops.segment_sum(src, seg, n)
kernel_name = 'mk_dlrm_tower_d1_rec_r8_cf1030'

def setup_inputs(seed: int=0):
    np.random.seed(seed)
    _w = jnp.asarray

    def _rec_inputs():
        import jax
        import jax.numpy as jnp
        _tk = jax.random.key(seed)
        ids = jnp.stack([jax.random.randint(jax.random.fold_in(_tk, 200 + f), (2048,), 0, v, jnp.int32) for f, v in enumerate([125000, 1000, 1250, 12500, 1000, 1250, 12500, 1250, 1250, 1250, 1250, 1250, 12500, 12500, 1000, 1250, 1250, 1250, 12500, 1250, 12500, 1000, 1000, 1250, 12500, 12500])], axis=1)
        tbl_0 = 0.05 * jax.random.normal(jax.random.fold_in(_tk, 500 + 0), (125000, 128), jnp.float32)
        tbl_1 = 0.05 * jax.random.normal(jax.random.fold_in(_tk, 500 + 1), (1000, 128), jnp.float32)
        tbl_2 = 0.05 * jax.random.normal(jax.random.fold_in(_tk, 500 + 2), (1250, 128), jnp.float32)
        tbl_3 = 0.05 * jax.random.normal(jax.random.fold_in(_tk, 500 + 3), (12500, 128), jnp.float32)
        tbl_4 = 0.05 * jax.random.normal(jax.random.fold_in(_tk, 500 + 4), (1000, 128), jnp.float32)
        tbl_5 = 0.05 * jax.random.normal(jax.random.fold_in(_tk, 500 + 5), (1250, 128), jnp.float32)
        tbl_6 = 0.05 * jax.random.normal(jax.random.fold_in(_tk, 500 + 6), (12500, 128), jnp.float32)
        tbl_7 = 0.05 * jax.random.normal(jax.random.fold_in(_tk, 500 + 7), (1250, 128), jnp.float32)
        tbl_8 = 0.05 * jax.random.normal(jax.random.fold_in(_tk, 500 + 8), (1250, 128), jnp.float32)
        tbl_9 = 0.05 * jax.random.normal(jax.random.fold_in(_tk, 500 + 9), (1250, 128), jnp.float32)
        tbl_10 = 0.05 * jax.random.normal(jax.random.fold_in(_tk, 500 + 10), (1250, 128), jnp.float32)
        tbl_11 = 0.05 * jax.random.normal(jax.random.fold_in(_tk, 500 + 11), (1250, 128), jnp.float32)
        tbl_12 = 0.05 * jax.random.normal(jax.random.fold_in(_tk, 500 + 12), (12500, 128), jnp.float32)
        tbl_13 = 0.05 * jax.random.normal(jax.random.fold_in(_tk, 500 + 13), (12500, 128), jnp.float32)
        tbl_14 = 0.05 * jax.random.normal(jax.random.fold_in(_tk, 500 + 14), (1000, 128), jnp.float32)
        tbl_15 = 0.05 * jax.random.normal(jax.random.fold_in(_tk, 500 + 15), (1250, 128), jnp.float32)
        tbl_16 = 0.05 * jax.random.normal(jax.random.fold_in(_tk, 500 + 16), (1250, 128), jnp.float32)
        tbl_17 = 0.05 * jax.random.normal(jax.random.fold_in(_tk, 500 + 17), (1250, 128), jnp.float32)
        tbl_18 = 0.05 * jax.random.normal(jax.random.fold_in(_tk, 500 + 18), (12500, 128), jnp.float32)
        tbl_19 = 0.05 * jax.random.normal(jax.random.fold_in(_tk, 500 + 19), (1250, 128), jnp.float32)
        tbl_20 = 0.05 * jax.random.normal(jax.random.fold_in(_tk, 500 + 20), (12500, 128), jnp.float32)
        tbl_21 = 0.05 * jax.random.normal(jax.random.fold_in(_tk, 500 + 21), (1000, 128), jnp.float32)
        tbl_22 = 0.05 * jax.random.normal(jax.random.fold_in(_tk, 500 + 22), (1000, 128), jnp.float32)
        tbl_23 = 0.05 * jax.random.normal(jax.random.fold_in(_tk, 500 + 23), (1250, 128), jnp.float32)
        tbl_24 = 0.05 * jax.random.normal(jax.random.fold_in(_tk, 500 + 24), (12500, 128), jnp.float32)
        tbl_25 = 0.05 * jax.random.normal(jax.random.fold_in(_tk, 500 + 25), (12500, 128), jnp.float32)
        _rk = jax.random.fold_in(_tk, 7)
        r_dense_output = -0.000520686 + 1.00062 * jax.random.normal(jax.random.fold_in(_rk, 101), (2048, 128), jnp.float32)
        W_top1 = 0.0405887 * jax.random.normal(jax.random.fold_in(_tk, 801), (607, 512), jnp.float32)
        W_top2 = 0.0441942 * jax.random.normal(jax.random.fold_in(_tk, 802), (512, 256), jnp.float32)
        W_top3 = 0.0625 * jax.random.normal(jax.random.fold_in(_tk, 803), (256, 1), jnp.float32)
        b_top1 = jnp.zeros((512,), jnp.float32)
        b_top2 = jnp.zeros((256,), jnp.float32)
        return (r_dense_output, ids, tbl_0, tbl_1, tbl_2, tbl_3, tbl_4, tbl_5, tbl_6, tbl_7, tbl_8, tbl_9, tbl_10, tbl_11, tbl_12, tbl_13, tbl_14, tbl_15, tbl_16, tbl_17, tbl_18, tbl_19, tbl_20, tbl_21, tbl_22, tbl_23, tbl_24, tbl_25, W_top1, b_top1, W_top2, b_top2, W_top3)
    r_dense_output, ids, tbl_0, tbl_1, tbl_2, tbl_3, tbl_4, tbl_5, tbl_6, tbl_7, tbl_8, tbl_9, tbl_10, tbl_11, tbl_12, tbl_13, tbl_14, tbl_15, tbl_16, tbl_17, tbl_18, tbl_19, tbl_20, tbl_21, tbl_22, tbl_23, tbl_24, tbl_25, W_top1, b_top1, W_top2, b_top2, W_top3 = _rec_inputs()

    def _L0_rec_setup():
        import jax, jax.numpy as jnp
        import numpy as np
        B, NUM_SPARSE, D = (2048, 26, 128)
        key = jax.random.key(seed)
        k1, k2 = jax.random.split(key)
        dense_output = jax.random.normal(k1, (B, D), dtype=jnp.float32)
        embeddings = jax.random.normal(k2, (B, NUM_SPARSE, D), dtype=jnp.float32)
        return {'dense_output': dense_output, 'embeddings': embeddings}
    _L0_rec_all = _L0_rec_setup()
    _L0_rec_in = {k: v for k, v in _L0_rec_all.items() if k in ()}
    del _L0_rec_all
    return {'r_dense_output': r_dense_output, 'ids': ids, 'tbl_0': tbl_0, 'tbl_1': tbl_1, 'tbl_2': tbl_2, 'tbl_3': tbl_3, 'tbl_4': tbl_4, 'tbl_5': tbl_5, 'tbl_6': tbl_6, 'tbl_7': tbl_7, 'tbl_8': tbl_8, 'tbl_9': tbl_9, 'tbl_10': tbl_10, 'tbl_11': tbl_11, 'tbl_12': tbl_12, 'tbl_13': tbl_13, 'tbl_14': tbl_14, 'tbl_15': tbl_15, 'tbl_16': tbl_16, 'tbl_17': tbl_17, 'tbl_18': tbl_18, 'tbl_19': tbl_19, 'tbl_20': tbl_20, 'tbl_21': tbl_21, 'tbl_22': tbl_22, 'tbl_23': tbl_23, 'tbl_24': tbl_24, 'tbl_25': tbl_25, 'W_top1': W_top1, 'b_top1': b_top1, 'W_top2': W_top2, 'b_top2': b_top2, 'W_top3': W_top3}

def reference(r_dense_output, ids, tbl_0, tbl_1, tbl_2, tbl_3, tbl_4, tbl_5, tbl_6, tbl_7, tbl_8, tbl_9, tbl_10, tbl_11, tbl_12, tbl_13, tbl_14, tbl_15, tbl_16, tbl_17, tbl_18, tbl_19, tbl_20, tbl_21, tbl_22, tbl_23, tbl_24, tbl_25, W_top1, b_top1, W_top2, b_top2, W_top3):
    import jax
    import jax.numpy as jnp

    def _L0_rec_ref(dense_output, embeddings):
        import jax, jax.numpy as jnp
        import numpy as np
        B, NUM_SPARSE, D = (2048, 26, 128)
        combined = jnp.concatenate([dense_output[:, None, :], embeddings], axis=1)
        interactions = jnp.einsum('bfd,bgd->bfg', combined, combined)
        F = combined.shape[1]
        iu, ju = jnp.triu_indices(F, k=1)
        interactions_flat = interactions[:, iu, ju]
        return jnp.concatenate([dense_output, interactions_flat], axis=1)
    e = jnp.stack([tbl_0[ids[:, 0]], tbl_1[ids[:, 1]], tbl_2[ids[:, 2]], tbl_3[ids[:, 3]], tbl_4[ids[:, 4]], tbl_5[ids[:, 5]], tbl_6[ids[:, 6]], tbl_7[ids[:, 7]], tbl_8[ids[:, 8]], tbl_9[ids[:, 9]], tbl_10[ids[:, 10]], tbl_11[ids[:, 11]], tbl_12[ids[:, 12]], tbl_13[ids[:, 13]], tbl_14[ids[:, 14]], tbl_15[ids[:, 15]], tbl_16[ids[:, 16]], tbl_17[ids[:, 17]], tbl_18[ids[:, 18]], tbl_19[ids[:, 19]], tbl_20[ids[:, 20]], tbl_21[ids[:, 21]], tbl_22[ids[:, 22]], tbl_23[ids[:, 23]], tbl_24[ids[:, 24]], tbl_25[ids[:, 25]]], axis=1)
    z = _L0_rec_ref(r_dense_output, e)
    z = z.reshape(z.shape[0], -1)
    h = jnp.concatenate([z, r_dense_output], axis=1)
    h = jnp.maximum(h @ W_top1 + b_top1, 0.0)
    h = jnp.maximum(h @ W_top2 + b_top2, 0.0)
    y = h @ W_top3
    return y

_drawn_inputs = setup_inputs


def setup_inputs(seed=0):
    import zlib

    import numpy as np

    out = dict(_drawn_inputs(seed))
    spreads = {'b_top1': (0.0, 0.1), 'b_top2': (0.0, 0.1)}
    factors = {}
    for name, (base, spread) in spreads.items():
        noise = np.random.default_rng([zlib.crc32(name.encode()), seed]).standard_normal(out[name].shape)
        drawn = base * np.exp(spread * noise) if base else spread * noise
        out[name] = jnp.asarray(drawn.astype(out[name].dtype))
    for name, factor in factors.items():
        out[name] = (out[name] * factor).astype(out[name].dtype)
    return out
```

```python
from contextlib import ExitStack

import numpy as np

import concourse.bass as bass
from concourse import mybir

F32 = mybir.dt.float32
I32 = mybir.dt.int32
ALU = mybir.AluOpType
ACT = mybir.ActivationFunctionType

P = 128
BATCH = 2048
D = 128
TABLES = 26
F = TABLES + 1
H1, H2 = 512, 256
TILE = 128
CHUNK = 256
TILES = CHUNK // TILE
CHUNKS = BATCH // CHUNK
QUAD = 4
QUADS = -(-F // QUAD)
GROUP = 4
GF = GROUP * F
GROUPS = TILE // GROUP
BANK_GROUPS = 4
UNIT_GROUPS = 2 * BANK_GROUPS
UNITS = GROUPS // UNIT_GROUPS
BANK = 512

HALF = F // 2
RUNS = [(c, 0, F - 1) for c in range(1, HALF + 1)] + [(HALF + 1, 0, HALF)]
PAIRS = sum(n for _, _, n in RUNS)
KP = 117
KSTEPS = PAIRS // KP


def pair_runs():
    out, row = [], 0
    for c, f, n in RUNS:
        while n:
            take = min(n, KP - row % KP)
            out.append(((F + 1) * f + c, take, row // KP, row % KP))
            f, n, row = f + take, n - take, row + take
    return out


def pair_rows():
    index = {}
    for r in range(F):
        for s in range(r + 1, F):
            index[(r, s)] = D + len(index)
    rows = []
    for q, n, _, _ in pair_runs():
        for j in range(n):
            r, s = divmod(q + (F + 1) * j, F)
            rows.append(index[(min(r, s), max(r, s))])
    return rows


def build(nc, dense, ids, tables, w_pairs, w_dense, b1, w2, b2, w3, y_out):
    with ExitStack() as ctx:
        def sb(name, shape, dt=F32):
            return ctx.enter_context(nc.sbuf_tensor(name, shape, dt))

        def psum(name, shape):
            return ctx.enter_context(nc.psum_tensor(name, shape, F32))

        def sem(name):
            return ctx.enter_context(nc.semaphore(name))

        gram_dram = nc.dram_tensor("gram_scratch", (TILES, GROUP, F, F, GROUPS), F32, kind="Internal").ap()

        ident = sb("ident", [P, P])
        ids_sb = [sb(f"ids{t}", [P, TABLES], I32) for t in range(TILES)]
        rows_sb = [sb(f"rows{t}", [P, F, D]) for t in range(TILES)]
        feat_sb = [sb(f"feat{t}", [P, GROUPS, GROUP, F]) for t in range(TILES)]
        gram_sb = [sb(f"gram{t}", [GF, GF, GROUPS]) for t in range(TILES)]
        pairs_sb = sb("pairs", [KP, KSTEPS, CHUNK])
        dense_sb = sb("dense_t", [P, CHUNK])
        h1_sb = sb("h1", [P, H1 // P, CHUNK])
        h2_sb = sb("h2", [P, H2 // P, CHUNK])
        y_sb = sb("y", [1, BATCH])
        w_pairs_sb = sb("w_pairs_sb", [KP, KSTEPS, H1])
        w_dense_sb = sb("w_dense_sb", [P, 2, H1])
        w_dsum_sb = sb("w_dsum_sb", [P, H1])
        w2_sb = sb("w2_sb", [P, H1 // P, H2])
        w3_sb = sb("w3_sb", [P, H2 // P])
        b1_sb = sb("b1_sb", [P, H1 // P])
        b2_sb = sb("b2_sb", [P, H2 // P])

        turn_ps = [psum(f"turn{i}", [P, QUAD, TILE]) for i in range(2)]
        gram_ps = [psum(f"gramps{i}", [P, 2, BANK]) for i in range(2)]
        top_ps = [psum(f"top{i}", [P, BANK]) for i in range(2)]

        weights_in = sem("weights_in")
        ident_zero = sem("ident_zero")
        ident_ready = sem("ident_ready")
        ids_in = [sem(f"ids_in{t}") for t in range(TILES)]
        dense_in = [sem(f"dense_in{t}") for t in range(TILES)]
        gathered = [[sem(f"gathered{t}_{q}") for q in range(QUADS)] for t in range(TILES)]
        turned = sem("turned")
        feat_act = sem("feat_act")
        feat_dve = sem("feat_dve")
        gram_made = sem("gram_made")
        gram_act = sem("gram_act")
        gram_dve = sem("gram_dve")
        scratch_in = [sem(f"scratch_in{t}") for t in range(TILES)]
        pairs_in = sem("pairs_in")
        dense_copied = sem("dense_copied")
        top1_made = sem("top1_made")
        h1_ready = sem("h1_ready")
        top2_made = sem("top2_made")
        h2_ready = sem("h2_ready")
        top3_made = sem("top3_made")
        top_free = sem("top_free")
        y_written = sem("y_written")

        quad_of = [range(QUAD * q, min(QUAD * q + QUAD, F)) for q in range(QUADS)]
        tables_of = [[f for f in quad if f > 0] for quad in quad_of]
        act_quads = [q for q in range(QUADS) if q % 2 == 0]
        dve_quads = [q for q in range(QUADS) if q % 2 == 1]
        runs = pair_runs()
        NB1, NB2 = H1 // P, H2 // P

        def counts(engine, values):
            return {k: v if isinstance(v, int) else engine.to_reg(v) for k, v in values.items()}

        def feat_out(t, q):
            v = feat_sb[t][:, :, :, QUAD * q:QUAD * q + len(quad_of[q])]
            return v.rearrange("p n s f -> p f s n")

        def feat_in(q):
            return turn_ps[q % 2][:, 0:len(quad_of[q]), :].rearrange("p f (s n) -> p f s n", s=GROUP)

        def gram_out(t, u):
            v = gram_sb[t][:, :, u * UNIT_GROUPS:(u + 1) * UNIT_GROUPS]
            return v.rearrange("p q (b n) -> p b n q", b=2)

        def gram_in(u):
            return gram_ps[u % 2][0:GF, :, 0:BANK_GROUPS * GF].rearrange("p b (n q) -> p b n q", q=GF)

        block = ctx.enter_context(nc.Block())

        @block.sync
        def _(sp):
            def load_ids(t, c):
                sp.dma_start(ids_sb[t][:], ids[bass.ds(c * CHUNK + t * TILE, TILE), :]).then_inc(ids_in[t], 16)

            def load_dense(t, c):
                sp.dma_start(rows_sb[t][:, 0, :],
                             dense[bass.ds(c * CHUNK + t * TILE, TILE), :]).then_inc(dense_in[t], 16)

            def chunk(c, last):
                read = counts(sp, {0: 16 * len(runs) * (c + 1)})[0]
                landed = counts(sp, {n: 16 * n * (c + 1) for n in sorted({len(x) for x in tables_of})})
                for t in range(TILES):
                    if not last:
                        sp.wait_ge(ids_in[t], 16)
                        for q in range(QUADS):
                            sp.wait_ge(gathered[t][q], landed[len(tables_of[q])])
                        load_ids(t, c + 1)
                        sp.wait_ge(dense_in[t], 16)
                        sp.wait_ge(turned, QUADS * (TILES * c + t) + 1)
                        load_dense(t, c + 1)
                    sp.wait_ge(gram_act, UNITS // 2 * (TILES * c + t + 1))
                    sp.wait_ge(gram_dve, UNITS // 2 * (TILES * c + t + 1))
                    for s in range(GROUP):
                        sp.dma_start(gram_dram[t, s].rearrange("f g n -> f (g n)"),
                                     gram_sb[t][F * s:F * s + F, F * s:F * s + F, :]
                                     .rearrange("p g n -> p (g n)")).then_inc(scratch_in[t], 16)
                for t in range(TILES):
                    sp.wait_ge(scratch_in[t], 16 * GROUP)
                    sp.wait_ge(scratch_in[t], 16 * GROUP * (c + 1))
                if not isinstance(c, int) or c > 0:
                    sp.wait_ge(top1_made, NB1 * c)
                flat = gram_dram.rearrange("t s f g n -> (f g) (t s) n")
                for q, n, k, row in runs:
                    sp.dma_start(pairs_sb[row:row + n, k, :].rearrange("p (u n) -> p u n", n=GROUPS),
                                 flat[q:q + (F + 1) * (n - 1) + 1:F + 1]).then_inc(pairs_in, 16)
                sp.wait_ge(scratch_in[0], 16 * GROUP)
                sp.wait_ge(pairs_in, read)

            for t in range(TILES):
                load_ids(t, 0)
                load_dense(t, 0)
            sp.dma_start(w_pairs_sb[:], w_pairs.rearrange("(k p) n -> p k n", p=KP)).then_inc(weights_in, 16)
            sp.dma_start(w_dense_sb[:], w_dense.rearrange("(k p) n -> p k n", p=P)).then_inc(weights_in, 16)
            sp.dma_start(w2_sb[:], w2.rearrange("(k p) n -> p k n", p=P)).then_inc(weights_in, 16)
            sp.dma_start(w3_sb[:], w3).then_inc(weights_in, 16)
            sp.dma_start(b1_sb[:], b1).then_inc(weights_in, 16)
            sp.dma_start(b2_sb[:], b2).then_inc(weights_in, 16)
            chunk(0, False)
            with sp.Fori(1, CHUNKS - 1) as c:
                chunk(c, False)
            chunk(CHUNKS - 1, True)
            sp.wait_ge(top_free, 1 + CHUNKS)
            sp.dma_start(y_out, y_sb[:]).then_inc(y_written, 16)
            sp.wait_ge(y_written, 16)

        @block.gpsimd
        def _(pool):
            nc.gpsimd.memset(ident[:], 0.0).then_inc(ident_zero, 1)
            pool.wait_ge(ident_zero, 1)
            nc.gpsimd.affine_select(out=ident[:], in_=ident[:], compare_op=ALU.not_equal, fill=1.0, base=0,
                                    pattern=[[-1, P]], channel_multiplier=1).then_inc(ident_ready, 1)

            def chunk(c):
                for t in range(TILES):
                    pool.wait_ge(ids_in[t], 16 * (c + 1))
                    for q in range(QUADS):
                        if not isinstance(c, int) or c > 0:
                            freed = pool.to_reg(QUADS * (TILES * (c - 1) + t) + q + 1)
                            pool.wait_ge(ids_in[t], 16)
                            pool.wait_ge(turned, freed)
                        for f in tables_of[q]:
                            nc.gpsimd.indirect_dma_start(
                                out=rows_sb[t][:, f, :], out_offset=None, in_=tables[f - 1][:, :],
                                in_offset=bass.IndirectOffsetOnAxis(ap=ids_sb[t][:, f - 1:f], axis=0),
                            ).then_inc(gathered[t][q], 16)

            chunk(0)
            with pool.Fori(1, CHUNKS) as c:
                chunk(c)

        @block.tensor
        def _(pe):
            def transposes(t, c):
                for q in range(QUADS):
                    if q == 0:
                        pe.wait_ge(dense_in[t], 16 * (c + 1))
                    pe.wait_ge(gathered[t][q], 16 * len(tables_of[q]) * (c + 1))
                    tile = TILES * c + t
                    before = (len(act_quads) * tile if q % 2 == 0 else len(dve_quads) * tile) + q // 2
                    if not isinstance(before, int) or before > 0:
                        pe.wait_ge(feat_act if q % 2 == 0 else feat_dve, before)
                    for j, f in enumerate(quad_of[q]):
                        last = nc.tensor.transpose(turn_ps[q % 2][:, j, :], rows_sb[t][:, f, :], ident[:])
                    last.then_inc(turned, 1)

            def grams(t, c):
                tile = TILES * c + t
                pe.wait_ge(feat_act, len(act_quads) * (tile + 1))
                pe.wait_ge(feat_dve, len(dve_quads) * (tile + 1))
                for u in range(UNITS):
                    before = UNITS // 2 * tile + u // 2
                    if not isinstance(before, int) or before > 0:
                        pe.wait_ge(gram_act if u % 2 == 0 else gram_dve, before)
                    for j in range(UNIT_GROUPS):
                        x = feat_sb[t][:, u * UNIT_GROUPS + j].rearrange("p s f -> p (s f)")
                        at = j % BANK_GROUPS * GF
                        last = nc.tensor.matmul(gram_ps[u % 2][0:GF, j // BANK_GROUPS, at:at + GF], x, x,
                                                start=True, stop=True)
                    last.then_inc(gram_made, 1)

            def top(c):
                pe.wait_ge(pairs_in, 16 * len(runs) * (c + 1))
                pe.wait_ge(dense_copied, TILES * (c + 1))
                pe.wait_ge(top_free, c + 1)
                for m in range(NB1):
                    if m >= 2:
                        pe.wait_ge(h1_ready, NB1 * c + m - 1)
                    ps = top_ps[m % 2][:, 0:CHUNK]
                    for k in range(KSTEPS):
                        nc.tensor.matmul(ps, w_pairs_sb[:, k, P * m:P * m + P], pairs_sb[:, k, :],
                                         start=(k == 0), stop=False)
                    nc.tensor.matmul(ps, w_dsum_sb[:, P * m:P * m + P], dense_sb[:],
                                     start=False, stop=True).then_inc(top1_made, 1)
                pe.wait_ge(h1_ready, NB1 * (c + 1))
                for m in range(NB2):
                    ps = top_ps[m % 2][:, 0:CHUNK]
                    for k in range(NB1):
                        last = nc.tensor.matmul(ps, w2_sb[:, k, P * m:P * m + P], h1_sb[:, k, :],
                                                start=(k == 0), stop=(k == NB1 - 1))
                    last.then_inc(top2_made, 1)
                pe.wait_ge(h2_ready, NB2 * (c + 1))
                for k in range(NB2):
                    last = nc.tensor.matmul(top_ps[0][0:1, 0:CHUNK], w3_sb[:, k:k + 1], h2_sb[:, k, :],
                                            start=(k == 0), stop=(k == NB2 - 1))
                last.then_inc(top3_made, 1)

            pe.wait_ge(ident_ready, 1)
            for t in range(TILES):
                transposes(t, 0)
                grams(t, 0)
            pe.wait_ge(weights_in, 16 * 6)
            with pe.Fori(1, CHUNKS) as c:
                transposes(0, c)
                grams(0, c)
                top(c - 1)
                transposes(1, c)
                grams(1, c)
            top(CHUNKS - 1)

        @block.scalar
        def _(act):
            def tile_copies(t, c):
                tile = TILES * c + t
                if not isinstance(c, int) or c > 0:
                    act.wait_ge(dense_copied, TILES * (c - 1) + t + 1)
                for q in act_quads:
                    act.wait_ge(turned, QUADS * tile + q + 1)
                    nc.scalar.copy(feat_out(t, q), feat_in(q)).then_inc(feat_act, 1)
                if not isinstance(c, int) or c > 0:
                    act.wait_ge(scratch_in[t], 16 * GROUP * c)
                for u in range(0, UNITS, 2):
                    act.wait_ge(gram_made, UNITS * tile + u + 1)
                    nc.scalar.copy(gram_out(t, u), gram_in(u)).then_inc(gram_act, 1)

            def top(c):
                for m in range(NB1):
                    act.wait_ge(top1_made, NB1 * c + m + 1)
                    nc.scalar.activation(h1_sb[:, m, :], top_ps[m % 2][:, 0:CHUNK], ACT.Relu,
                                         bias=b1_sb[:, m:m + 1]).then_inc(h1_ready, 1)

            act.wait_ge(weights_in, 16 * 6)
            for t in range(TILES):
                tile_copies(t, 0)
            with act.Fori(1, CHUNKS) as c:
                tile_copies(0, c)
                top(c - 1)
                tile_copies(1, c)
            top(CHUNKS - 1)

        @block.vector
        def _(dve):
            def tile_copies(t, c):
                tile = TILES * c + t
                for q in dve_quads:
                    dve.wait_ge(turned, QUADS * tile + q + 1)
                    nc.vector.tensor_copy(feat_out(t, q), feat_in(q)).then_inc(feat_dve, 1)
                if not isinstance(c, int) or c > 0:
                    dve.wait_ge(scratch_in[t], 16 * GROUP * c)
                for u in range(1, UNITS, 2):
                    dve.wait_ge(gram_made, UNITS * tile + u + 1)
                    nc.vector.tensor_copy(gram_out(t, u), gram_in(u)).then_inc(gram_dve, 1)

            def dense_copies(c):
                dve.wait_ge(feat_act, len(act_quads) * TILES * (c + 1))
                for t in range(TILES):
                    nc.vector.tensor_copy(
                        dense_sb[:, TILE * t:TILE * t + TILE].rearrange("p (s n) -> p s n", s=GROUP),
                        feat_sb[t][:, :, :, 0].rearrange("p n s -> p s n")).then_inc(dense_copied, 1)

            def top(c):
                for m in range(NB2):
                    dve.wait_ge(top2_made, NB2 * c + m + 1)
                    nc.vector.tensor_scalar(h2_sb[:, m, :], top_ps[m % 2][:, 0:CHUNK], b2_sb[:, m:m + 1], 0.0,
                                            ALU.add, ALU.max).then_inc(h2_ready, 1)
                dve.wait_ge(top3_made, c + 1)
                nc.vector.tensor_copy(y_sb[:, bass.ds(c * CHUNK, CHUNK)],
                                      top_ps[0][0:1, 0:CHUNK]).then_inc(top_free, 1)

            dve.wait_ge(weights_in, 16 * 6)
            nc.vector.tensor_tensor(w_dsum_sb[:], w_dense_sb[:, 0, :], w_dense_sb[:, 1, :],
                                    ALU.add).then_inc(top_free, 1)
            for t in range(TILES):
                tile_copies(t, 0)
            dense_copies(0)
            with dve.Fori(1, CHUNKS) as c:
                tile_copies(0, c)
                top(c - 1)
                tile_copies(1, c)
                dense_copies(c)
            top(CHUNKS - 1)


def kernel(**inputs):
    import concourse.bacc as bacc
    from concourse.bass_utils import run_bass_kernel_spmd

    w1 = np.asarray(inputs["W_top1"])
    arrays = {
        "dense": np.ascontiguousarray(inputs["r_dense_output"]),
        "ids": np.ascontiguousarray(inputs["ids"]),
        "w_pairs": np.ascontiguousarray(w1[np.array(pair_rows())]),
        "w_dense": np.concatenate([w1[:D], w1[D + PAIRS:]]),
        "b1": np.ascontiguousarray(np.asarray(inputs["b_top1"]).reshape(-1, P).T),
        "w2": np.ascontiguousarray(inputs["W_top2"]),
        "b2": np.ascontiguousarray(np.asarray(inputs["b_top2"]).reshape(-1, P).T),
        "w3": np.ascontiguousarray(np.asarray(inputs["W_top3"]).reshape(-1, P).T),
    }
    for f in range(TABLES):
        arrays[f"tbl_{f}"] = np.ascontiguousarray(inputs[f"tbl_{f}"])
    nc = bacc.Bacc("TRN2", target_bir_lowering=False, num_devices=1)
    ap = {n: nc.dram_tensor(n, a.shape, mybir.dt.from_np(a.dtype), kind="ExternalInput").ap()
          for n, a in arrays.items()}
    y = nc.dram_tensor("y_out", (1, BATCH), F32, kind="ExternalOutput").ap()
    build(nc, ap["dense"], ap["ids"], [ap[f"tbl_{f}"] for f in range(TABLES)], ap["w_pairs"], ap["w_dense"],
          ap["b1"], ap["w2"], ap["b2"], ap["w3"], y)
    result = run_bass_kernel_spmd(nc, [arrays], core_ids=[0])
    return result.results[0]["y_out"].reshape(BATCH, 1)
```

```python
from contextlib import ExitStack

import numpy as np

import concourse.bass as bass
from concourse import mybir

F32 = mybir.dt.float32
F32R = mybir.dt.float32r
I32 = mybir.dt.int32
ALU = mybir.AluOpType
ACT = mybir.ActivationFunctionType

P = 128
BATCH = 2048
D = 128
VOCAB = [125000, 1000, 1250, 12500, 1000, 1250, 12500, 1250, 1250, 1250, 1250, 1250, 12500,
         12500, 1000, 1250, 1250, 1250, 12500, 1250, 12500, 1000, 1000, 1250, 12500, 12500]
TABLES = len(VOCAB)
F = TABLES + 1
H1, H2 = 512, 256

PICKED = sorted(range(TABLES), key=lambda f: VOCAB[f])[:7]
GATHERED = [f for f in range(TABLES) if f not in PICKED]
RP = 125
BLOCKS = [VOCAB[f] // RP for f in PICKED]
MAX_BLOCKS = max(BLOCKS)
ORDER = GATHERED + PICKED
TURNED = 1 + len(GATHERED)

TILE = 128
CHUNK = 256
TILES = CHUNK // TILE
CHUNKS = BATCH // CHUNK
QUAD = 4
QUADS = TURNED // QUAD
GROUP = 4
GF = GROUP * F
GROUPS = TILE // GROUP
UNIT = 4
UNITS = GROUPS // UNIT
BANK = 512
NPICK = len(PICKED)
PAIRS_PICKED = -(-NPICK // 2)
STAGED = 4
HOTS = 3

HALF = F // 2
OFFSETS = [(c, 0, F - 1) for c in range(1, HALF + 1)] + [(HALF + 1, 0, HALF)]
PAIRS = sum(n for _, _, n in OFFSETS)
KP = 117
KSTEPS = PAIRS // KP

assert TURNED % QUAD == 0 and GROUPS % UNIT == 0 and UNITS % 2 == 0 and PAIRS_PICKED % 2 == 0
assert PAIRS == KP * KSTEPS and all(VOCAB[f] % RP == 0 for f in PICKED)


def pair_runs():
    out, row = [], 0
    for c, f, n in OFFSETS:
        while n:
            take = min(n, KP - row % KP)
            out.append(((F + 1) * f + c, take, row // KP, row % KP))
            f, n, row = f + take, n - take, row + take
    return out


def pair_rows():
    index = {}
    for r in range(F):
        for s in range(r + 1, F):
            index[(r, s)] = D + len(index)
    feature = [0] + [f + 1 for f in ORDER]
    rows = []
    for q, n, _, _ in pair_runs():
        for j in range(n):
            r, s = divmod(q + (F + 1) * j, F)
            rows.append(index[tuple(sorted((feature[r], feature[s])))])
    return rows


def build(nc, dense, ids, ids_t, tables, w_pairs, w_dense, b1, w2, b2, w3, y_out):
    with ExitStack() as ctx:
        def sb(name, shape, dt=F32):
            return ctx.enter_context(nc.sbuf_tensor(name, shape, dt))

        def psum(name, shape):
            return ctx.enter_context(nc.psum_tensor(name, shape, F32))

        def sem(name):
            return ctx.enter_context(nc.semaphore(name))

        gram_dram = nc.dram_tensor("gram_scratch", (TILES, GROUP, F, F, GROUPS), F32, kind="Internal").ap()

        ident = sb("ident", [P, P])
        ids_sb = [sb(f"ids{t}", [P, TABLES], I32) for t in range(TILES)]
        rows_sb = [sb(f"rows{t}", [P, TURNED, D]) for t in range(TILES)]
        feat_sb = [sb(f"feat{t}", [P, GROUPS, GROUP, F]) for t in range(TILES)]
        gram_sb = [sb(f"gram{t}", [P, GF, GROUPS]) for t in range(TILES)]
        table_sb = [sb(f"table{i}", [RP, 2, BLOCKS[i], D], F32R) for i in range(NPICK)]
        picks_sb = sb("picks", [RP, NPICK, CHUNK], I32)
        row_id = {n: sb(f"row_id{n}", [P, n], I32) for n in sorted(set(BLOCKS))}
        hot_sb = [sb(f"hot{i}", [RP, MAX_BLOCKS, CHUNK], F32R) for i in range(HOTS)]
        pairs_sb = sb("pairs", [KP, KSTEPS, CHUNK])
        dense_sb = sb("dense_t", [P, CHUNK])
        h1_sb = sb("h1", [P, H1 // P, CHUNK])
        h2_sb = sb("h2", [P, H2 // P, CHUNK])
        y_sb = sb("y", [P, BATCH // TILE])
        y_rows = sb("y_rows", [BATCH // TILE, TILE])
        w_pairs_sb = sb("w_pairs_sb", [KP, KSTEPS, H1])
        w_dense_sb = sb("w_dense_sb", [P, 2, H1])
        w_dsum_sb = sb("w_dsum_sb", [P, H1])
        w2_sb = sb("w2_sb", [P, H1 // P, H2])
        w3_sb = sb("w3_sb", [P, H2 // P])
        b1_sb = sb("b1_sb", [P, H1 // P])
        b2_sb = sb("b2_sb", [P, H2 // P])

        turn_ps = [psum(f"turn{i}", [P, QUAD, TILE]) for i in range(2)]
        gram_ps = [psum(f"gramps{i}", [P, BANK]) for i in range(2)]
        pick_ps = [psum(f"pickps{i}", [P, 2, CHUNK]) for i in range(2)]
        top_ps = [psum(f"top{i}", [P, BANK]) for i in range(2)]

        weights_in = sem("weights_in")
        ident_zero = sem("ident_zero")
        ident_ready = sem("ident_ready")
        staged = [sem(f"staged{i}") for i in range(STAGED)]
        split_high = sem("split_high")
        split_low = sem("split_low")
        ids_in = [sem(f"ids_in{t}") for t in range(TILES)]
        picks_in = sem("picks_in")
        dense_in = [sem(f"dense_in{t}") for t in range(TILES)]
        gathered = [[sem(f"gathered{t}_{q}") for q in range(QUADS)] for t in range(TILES)]
        turned = sem("turned")
        feat_act = sem("feat_act")
        feat_dve = sem("feat_dve")
        hot_made = sem("hot_made")
        picked = sem("picked")
        pick_out = sem("pick_out")
        gram_made = sem("gram_made")
        gram_out = sem("gram_out")
        scratch_in = [sem(f"scratch_in{t}") for t in range(TILES)]
        pairs_in = sem("pairs_in")
        dense_copied = sem("dense_copied")
        top1_made = sem("top1_made")
        h1_ready = sem("h1_ready")
        top2_made = sem("top2_made")
        h2_ready = sem("h2_ready")
        top3_made = sem("top3_made")
        top_free = sem("top_free")
        y_turned = sem("y_turned")
        y_ready = sem("y_ready")
        y_written = sem("y_written")

        NB1, NB2 = H1 // P, H2 // P
        WEIGHTS = 6
        ACT_QUADS, DVE_QUADS = (QUADS + 1) // 2, QUADS // 2
        runs = pair_runs()

        def slots_of(q):
            return [f for f in range(QUAD * q, QUAD * q + QUAD) if f > 0]

        def started(c):
            return not isinstance(c, int) or c > 0

        def feat_out(t, q):
            return feat_sb[t][:, :, :, QUAD * q:QUAD * q + QUAD].rearrange("p n s f -> p f s n")

        def feat_in(q):
            return turn_ps[q % 2][:].rearrange("p f (s n) -> p f s n", s=GROUP)

        def last_user(i):
            return max(k for k in range(NPICK) if k % HOTS == i % HOTS)

        def stage(i, n):
            flat = gram_sb[i % STAGED // 2].rearrange("p q n -> p (q n)")
            at = i % 2 * MAX_BLOCKS * D
            return flat[0:RP, at:at + n * D].rearrange("p (j d) -> p j d", d=D)

        block = ctx.enter_context(nc.Block())

        @block.sync
        def _(sp):
            def load_ids(t, c):
                sp.dma_start(ids_sb[t][:], ids[bass.ds(c * CHUNK + t * TILE, TILE), :]).then_inc(ids_in[t], 16)

            def load_dense(t, c):
                sp.dma_start(rows_sb[t][:, 0, :],
                             dense[bass.ds(c * CHUNK + t * TILE, TILE), :]).then_inc(dense_in[t], 16)

            def load_picks(c):
                sp.dma_start(picks_sb[:], ids_t[:, bass.ds(c * CHUNK, CHUNK)].unsqueeze(0)
                             .to_broadcast([RP, NPICK, CHUNK])).then_inc(picks_in, 16)

            def load_table(i):
                sp.dma_start(stage(i, BLOCKS[i]), tables[PICKED[i]].rearrange("(p j) d -> p j d", p=RP)
                             ).then_inc(staged[i % STAGED], 16)

            def next_tile(t, c):
                landed = sp.to_reg(16 * QUAD * c) if started(c - 1) else 16 * QUAD
                landed0 = sp.to_reg(16 * (QUAD - 1) * c) if started(c - 1) else 16 * (QUAD - 1)
                sp.wait_ge(ids_in[t], 16)
                for q in range(1, QUADS):
                    sp.wait_ge(gathered[t][q], landed)
                sp.wait_ge(gathered[t][0], landed0)
                load_ids(t, c)
                freed = QUADS * (TILES * (c - 1) + t) + 1
                if started(c - 1):
                    freed = sp.to_reg(freed)
                sp.wait_ge(dense_in[t], 16)
                sp.wait_ge(turned, freed)
                load_dense(t, c)

            def next_picks(c):
                made = NPICK * c if isinstance(c, int) else sp.to_reg(NPICK * c)
                sp.wait_ge(picks_in, 16)
                sp.wait_ge(hot_made, made)
                load_picks(c)

            def write_gram(t, c):
                sp.wait_ge(gram_out, UNITS * (TILES * c + t + 1))
                for s in range(GROUP):
                    sp.dma_start(gram_dram[t, s].rearrange("f g n -> f (g n)"),
                                 gram_sb[t][F * s:F * s + F, F * s:F * s + F, :]
                                 .rearrange("p g n -> p (g n)")).then_inc(scratch_in[t], 16)

            def read_pairs(c):
                for t in range(TILES):
                    sp.wait_ge(scratch_in[t], 16 * GROUP)
                    sp.wait_ge(scratch_in[t], 16 * GROUP * (c + 1))
                flat = gram_dram.rearrange("t s f g n -> (f g) (t s) n")
                for q, n, k, row in runs:
                    sp.dma_start(pairs_sb[row:row + n, k, :].rearrange("p (u n) -> p u n", n=GROUPS),
                                 flat[q:q + (F + 1) * (n - 1) + 1:F + 1]).then_inc(pairs_in, 16)

            def chunk(c, last):
                read = 16 * len(runs) * c if isinstance(c, int) else sp.to_reg(16 * len(runs) * c)
                write_gram(1, c - 1)
                read_pairs(c - 1)
                if not last:
                    next_tile(0, c + 1)
                    next_picks(c + 1)
                    next_tile(1, c + 1)
                sp.wait_ge(scratch_in[0], 16)
                sp.wait_ge(pairs_in, read)
                write_gram(0, c)

            load_ids(0, 0)
            load_picks(0)
            load_table(0)
            load_table(1)
            load_ids(1, 0)
            load_table(2)
            load_table(3)
            load_dense(0, 0)
            for i in range(STAGED, NPICK):
                sp.wait_ge(split_low, i - STAGED + 1)
                load_table(i)
            load_dense(1, 0)
            sp.dma_start(w_pairs_sb[:], w_pairs.rearrange("(k p) n -> p k n", p=KP)).then_inc(weights_in, 16)
            sp.dma_start(w_dense_sb[:], w_dense.rearrange("(k p) n -> p k n", p=P)).then_inc(weights_in, 16)
            sp.dma_start(w2_sb[:], w2.rearrange("(k p) n -> p k n", p=P)).then_inc(weights_in, 16)
            sp.dma_start(w3_sb[:], w3).then_inc(weights_in, 16)
            sp.dma_start(b1_sb[:], b1).then_inc(weights_in, 16)
            sp.dma_start(b2_sb[:], b2).then_inc(weights_in, 16)
            next_picks(1)
            next_tile(0, 1)
            write_gram(0, 0)
            next_tile(1, 1)
            with sp.Fori(1, CHUNKS - 1) as c:
                chunk(c, False)
            chunk(CHUNKS - 1, True)
            write_gram(1, CHUNKS - 1)
            read_pairs(CHUNKS - 1)
            sp.wait_ge(y_ready, 1)
            sp.dma_start(y_out, y_rows[:]).then_inc(y_written, 16)
            sp.wait_ge(y_written, 16)

        @block.gpsimd
        def _(pool):
            def chunk(c):
                for t in range(TILES):
                    pool.wait_ge(ids_in[t], 16 * (c + 1))
                    for q in range(QUADS):
                        if started(c):
                            freed = pool.to_reg(QUADS * (TILES * (c - 1) + t) + q + 1)
                            pool.wait_ge(ids_in[t], 16)
                            pool.wait_ge(turned, freed)
                        for f in slots_of(q):
                            table = ORDER[f - 1]
                            nc.gpsimd.indirect_dma_start(
                                out=rows_sb[t][:, f, :], out_offset=None, in_=tables[table][:, :],
                                in_offset=bass.IndirectOffsetOnAxis(ap=ids_sb[t][:, table:table + 1], axis=0),
                            ).then_inc(gathered[t][q], 16)

            for n in row_id:
                nc.gpsimd.iota(row_id[n][:], pattern=[[1, n]], base=0, channel_multiplier=n).then_inc(ident_ready, 1)
            nc.gpsimd.memset(ident[:], 0.0).then_inc(ident_zero, 1)
            pool.wait_ge(ident_zero, 1)
            nc.gpsimd.affine_select(out=ident[:], in_=ident[:], compare_op=ALU.not_equal, fill=1.0, base=0,
                                    pattern=[[-1, P]], channel_multiplier=1).then_inc(ident_ready, 1)
            chunk(0)
            with pool.Fori(1, CHUNKS) as c:
                chunk(c)

        @block.tensor
        def _(pe):
            def transposes(t, c, q):
                tile = TILES * c + t
                if q == 0:
                    pe.wait_ge(dense_in[t], 16 * (c + 1))
                pe.wait_ge(gathered[t][q], 16 * len(slots_of(q)) * (c + 1))
                before = (ACT_QUADS if q % 2 == 0 else DVE_QUADS) * tile + q // 2
                if not isinstance(before, int) or before > 0:
                    pe.wait_ge(feat_act if q % 2 == 0 else feat_dve, before)
                for j in range(QUAD):
                    last = nc.tensor.transpose(turn_ps[q % 2][:, j, :], rows_sb[t][:, QUAD * q + j, :], ident[:])
                last.then_inc(turned, 1)

            def pick(i, c):
                pe.wait_ge(hot_made, NPICK * c + i + 1)
                if not started(c):
                    pe.wait_ge(split_low, i + 1)
                before = PAIRS_PICKED * c + i // 2 - 1
                if i % 2 == 0 and (started(c) or before > 0):
                    pe.wait_ge(pick_out, before)
                for j in range(BLOCKS[i]):
                    for half in range(2):
                        last = nc.tensor.matmul(pick_ps[i // 2 % 2][:, i % 2, :], table_sb[i][:, half, j, :],
                                                hot_sb[i % HOTS][:, j, :], start=(j == 0 and half == 0),
                                                stop=(j == BLOCKS[i] - 1 and half == 1))
                last.then_inc(picked, 1)

            def gram(t, c, u):
                tile = TILES * c + t
                if u == 0:
                    pe.wait_ge(feat_act, ACT_QUADS * (tile + 1))
                    pe.wait_ge(feat_dve, DVE_QUADS * (tile + 1))
                    pe.wait_ge(pick_out, PAIRS_PICKED * (c + 1))
                before = UNITS * tile + u - 1
                if not isinstance(before, int) or before > 0:
                    pe.wait_ge(gram_out, before)
                for j in range(UNIT):
                    x = feat_sb[t][:, UNIT * u + j].rearrange("p s f -> p (s f)")
                    last = nc.tensor.matmul(gram_ps[u % 2][0:GF, GF * j:GF * j + GF], x, x, start=True, stop=True)
                last.then_inc(gram_made, 1)

            def layer1(c, m):
                if m == 0:
                    pe.wait_ge(pairs_in, 16 * len(runs) * (c + 1))
                    pe.wait_ge(dense_copied, TILES * (c + 1))
                    pe.wait_ge(top_free, c + 1)
                if m >= 2:
                    pe.wait_ge(h1_ready, NB1 * c + m - 1)
                ps = top_ps[m % 2][:, 0:CHUNK]
                for k in range(KSTEPS):
                    nc.tensor.matmul(ps, w_pairs_sb[:, k, P * m:P * m + P], pairs_sb[:, k, :],
                                     start=(k == 0), stop=False)
                nc.tensor.matmul(ps, w_dsum_sb[:, P * m:P * m + P], dense_sb[:],
                                 start=False, stop=True).then_inc(top1_made, 1)

            def layer2(c):
                pe.wait_ge(h1_ready, NB1 * (c + 1))
                for m in range(NB2):
                    ps = top_ps[m % 2][:, 0:CHUNK]
                    for k in range(NB1):
                        last = nc.tensor.matmul(ps, w2_sb[:, k, P * m:P * m + P], h1_sb[:, k, :],
                                                start=(k == 0), stop=(k == NB1 - 1))
                    last.then_inc(top2_made, 1)

            def layer3(c):
                pe.wait_ge(h2_ready, NB2 * (c + 1))
                for t in range(TILES):
                    for k in range(NB2):
                        last = nc.tensor.matmul(top_ps[0][:, t:t + 1], h2_sb[:, k, TILE * t:TILE * t + TILE],
                                                w3_sb[:, k:k + 1], start=(k == 0), stop=(k == NB2 - 1))
                last.then_inc(top3_made, 1)

            pe.wait_ge(ident_ready, 1 + len(row_id))
            for i in range(NPICK):
                pick(i, 0)
            for q in range(QUADS):
                transposes(0, 0, q)
            for u in range(UNITS):
                gram(0, 0, u)
            for q in range(QUADS):
                transposes(1, 0, q)
            pe.wait_ge(weights_in, 16 * WEIGHTS)
            with pe.Fori(1, CHUNKS) as c:
                for u in range(UNITS):
                    gram(1, c - 1, u)
                for i in range(NPICK):
                    pick(i, c)
                    if i > 0 and i <= QUADS:
                        transposes(0, c, i - 1)
                for m in range(NB1):
                    layer1(c - 1, m)
                layer2(c - 1)
                transposes(1, c, 0)
                transposes(1, c, 1)
                layer3(c - 1)
                for q in range(2, QUADS):
                    transposes(1, c, q)
                for u in range(UNITS):
                    gram(0, c, u)
            for u in range(UNITS):
                gram(1, CHUNKS - 1, u)
            for m in range(NB1):
                layer1(CHUNKS - 1, m)
            layer2(CHUNKS - 1)
            layer3(CHUNKS - 1)
            pe.wait_ge(top_free, 1 + CHUNKS)
            nc.tensor.transpose(top_ps[1][0:BATCH // TILE, 0:TILE], y_sb[:], ident[:]).then_inc(y_turned, 1)

        @block.scalar
        def _(act):
            def copy_quad(t, c, q):
                tile = TILES * c + t
                if q == 0 and started(c):
                    act.wait_ge(dense_copied, TILES * (c - 1) + t + 1)
                act.wait_ge(turned, QUADS * tile + q + 1)
                nc.scalar.copy(feat_out(t, q), feat_in(q)).then_inc(feat_act, 1)

            def copy_picked(k, c):
                n = min(2, NPICK - 2 * k)
                act.wait_ge(picked, NPICK * c + min(2 * k + 2, NPICK))
                for t in range(TILES):
                    at = TURNED + 2 * k
                    last = nc.scalar.copy(
                        feat_sb[t][:, :, :, at:at + n].rearrange("p n s f -> p f s n"),
                        pick_ps[k % 2][:, 0:n, TILE * t:TILE * t + TILE].rearrange("p f (s n) -> p f s n", s=GROUP))
                last.then_inc(pick_out, 1)

            def copy_gram(t, c, u):
                if u == 0 and started(c):
                    act.wait_ge(scratch_in[t], 16 * GROUP * c)
                if u == 0 and not started(c):
                    act.wait_ge(split_low, NPICK)
                act.wait_ge(gram_made, UNITS * (TILES * c + t) + u + 1)
                nc.scalar.copy(gram_sb[t][0:GF, :, UNIT * u:UNIT * u + UNIT].rearrange("p q n -> p n q"),
                               gram_ps[u % 2][0:GF, 0:UNIT * GF].rearrange("p (n q) -> p n q", q=GF)
                               ).then_inc(gram_out, 1)

            def layer1(c, m):
                act.wait_ge(top1_made, NB1 * c + m + 1)
                nc.scalar.activation(h1_sb[:, m, :], top_ps[m % 2][:, 0:CHUNK], ACT.Relu,
                                     bias=b1_sb[:, m:m + 1]).then_inc(h1_ready, 1)

            for i in range(NPICK):
                act.wait_ge(staged[i % STAGED], 16 * (i // STAGED + 1))
                nc.scalar.copy(table_sb[i][:, 0], stage(i, BLOCKS[i])).then_inc(split_high, 1)
            for k in range(PAIRS_PICKED):
                copy_picked(k, 0)
            act.wait_ge(weights_in, 16 * WEIGHTS)
            for q in range(0, QUADS, 2):
                copy_quad(0, 0, q)
            for u in range(UNITS):
                copy_gram(0, 0, u)
            for q in range(0, QUADS, 2):
                copy_quad(1, 0, q)
            with act.Fori(1, CHUNKS) as c:
                for u in range(UNITS):
                    copy_gram(1, c - 1, u)
                for i in range(NPICK):
                    if i % 2 == 1 or i == NPICK - 1:
                        copy_picked(i // 2, c)
                    if i > 0 and i <= QUADS and i % 2 == 1:
                        copy_quad(0, c, i - 1)
                for m in range(NB1):
                    layer1(c - 1, m)
                for q in range(0, QUADS, 2):
                    copy_quad(1, c, q)
                for u in range(UNITS):
                    copy_gram(0, c, u)
            for u in range(UNITS):
                copy_gram(1, CHUNKS - 1, u)
            for m in range(NB1):
                layer1(CHUNKS - 1, m)

        @block.vector
        def _(dve):
            def one_hot(i, c):
                if i == 0:
                    dve.wait_ge(picks_in, 16 * (c + 1))
                before = NPICK * (c - 1) + last_user(i) + 1 if i < HOTS else NPICK * c + i - HOTS + 1
                if started(c) or i >= HOTS:
                    dve.wait_ge(picked, before)
                for j in range(BLOCKS[i]):
                    last = nc.vector.tensor_scalar(hot_sb[i % HOTS][:, j, :], picks_sb[:, i, :],
                                                   row_id[BLOCKS[i]][0:RP, j:j + 1], None, ALU.is_equal)
                last.then_inc(hot_made, 1)

            def copy_quad(t, c, q):
                dve.wait_ge(turned, QUADS * (TILES * c + t) + q + 1)
                nc.vector.tensor_copy(feat_out(t, q), feat_in(q)).then_inc(feat_dve, 1)

            def dense_copies(c):
                dve.wait_ge(feat_act, ACT_QUADS * (TILES * c + 1) + 1)
                for t in range(TILES):
                    nc.vector.tensor_copy(
                        dense_sb[:, TILE * t:TILE * t + TILE].rearrange("p (s n) -> p s n", s=GROUP),
                        feat_sb[t][:, :, :, 0].rearrange("p n s -> p s n")).then_inc(dense_copied, 1)

            def layer2(c):
                for m in range(NB2):
                    dve.wait_ge(top2_made, NB2 * c + m + 1)
                    nc.vector.tensor_scalar(h2_sb[:, m, :], top_ps[m % 2][:, 0:CHUNK], b2_sb[:, m:m + 1], 0.0,
                                            ALU.add, ALU.max).then_inc(h2_ready, 1)

            def layer3(c):
                dve.wait_ge(top3_made, c + 1)
                nc.vector.tensor_copy(y_sb[:, bass.ds(c * TILES, TILES)],
                                      top_ps[0][:, 0:TILES]).then_inc(top_free, 1)

            def chunk(c, last):
                for i in range(HOTS, NPICK):
                    one_hot(i, c)
                    if i % 2 == 0:
                        copy_quad(0, c, i - HOTS)
                layer2(c - 1)
                copy_quad(1, c, 1)
                layer3(c - 1)
                copy_quad(1, c, 3)
                dense_copies(c)
                if not last:
                    for i in range(HOTS):
                        one_hot(i, c + 1)

            dve.wait_ge(ident_ready, 1 + len(row_id))
            for i in range(NPICK):
                dve.wait_ge(split_high, i + 1)
                nc.vector.tensor_tensor(table_sb[i][:, 1], stage(i, BLOCKS[i]), table_sb[i][:, 0],
                                        ALU.subtract).then_inc(split_low, 1)
                one_hot(i, 0)
            dve.wait_ge(weights_in, 16 * WEIGHTS)
            nc.vector.tensor_tensor(w_dsum_sb[:], w_dense_sb[:, 0, :], w_dense_sb[:, 1, :],
                                    ALU.add).then_inc(top_free, 1)
            for q in range(1, QUADS, 2):
                copy_quad(0, 0, q)
            for i in range(HOTS):
                one_hot(i, 1)
            for q in range(1, QUADS, 2):
                copy_quad(1, 0, q)
            dense_copies(0)
            with dve.Fori(1, CHUNKS - 1) as c:
                chunk(c, False)
            chunk(CHUNKS - 1, True)
            layer2(CHUNKS - 1)
            layer3(CHUNKS - 1)
            dve.wait_ge(y_turned, 1)
            nc.vector.tensor_copy(y_rows[:], top_ps[1][0:BATCH // TILE, 0:TILE]).then_inc(y_ready, 1)


def kernel(**inputs):
    import concourse.bacc as bacc
    from concourse.bass_utils import run_bass_kernel_spmd

    def column_blocks(a):
        return np.ascontiguousarray(np.asarray(a).reshape(-1, P).T)

    w1 = np.asarray(inputs["W_top1"])
    ids = np.ascontiguousarray(inputs["ids"])
    arrays = {
        "dense": np.ascontiguousarray(inputs["r_dense_output"]),
        "ids": ids,
        "ids_t": np.ascontiguousarray(ids.T[PICKED]),
        "w_pairs": np.ascontiguousarray(w1[np.array(pair_rows())]),
        "w_dense": np.concatenate([w1[:D], w1[D + PAIRS:]]),
        "b1": column_blocks(inputs["b_top1"]),
        "w2": np.ascontiguousarray(inputs["W_top2"]),
        "b2": column_blocks(inputs["b_top2"]),
        "w3": column_blocks(inputs["W_top3"]),
    }
    for f in range(TABLES):
        arrays[f"tbl_{f}"] = np.ascontiguousarray(inputs[f"tbl_{f}"])
    nc = bacc.Bacc("TRN2", target_bir_lowering=False, num_devices=1)
    ap = {n: nc.dram_tensor(n, a.shape, mybir.dt.from_np(a.dtype), kind="ExternalInput").ap()
          for n, a in arrays.items()}
    y = nc.dram_tensor("y_out", (BATCH // TILE, TILE), F32, kind="ExternalOutput").ap()
    build(nc, ap["dense"], ap["ids"], ap["ids_t"], [ap[f"tbl_{f}"] for f in range(TABLES)], ap["w_pairs"],
          ap["w_dense"], ap["b1"], ap["w2"], ap["b2"], ap["w3"], y)
    result = run_bass_kernel_spmd(nc, [arrays], core_ids=[0])
    return result.results[0]["y_out"].reshape(BATCH, 1)
```

```python
from contextlib import ExitStack

import numpy as np

import concourse.bass as bass
from concourse import mybir

F32 = mybir.dt.float32
F32R = mybir.dt.float32r
I32 = mybir.dt.int32
ALU = mybir.AluOpType
ACT = mybir.ActivationFunctionType

P = 128
BATCH = 2048
D = 128
VOCAB = [125000, 1000, 1250, 12500, 1000, 1250, 12500, 1250, 1250, 1250, 1250, 1250, 12500,
         12500, 1000, 1250, 1250, 1250, 12500, 1250, 12500, 1000, 1000, 1250, 12500, 12500]
TABLES = len(VOCAB)
F = TABLES + 1
H1, H2 = 512, 256

PICKED = sorted(range(TABLES), key=lambda f: VOCAB[f])[:7]
GATHERED = [f for f in range(TABLES) if f not in PICKED]
RP = 125
BLOCKS = [VOCAB[f] // RP for f in PICKED]
MAX_BLOCKS = max(BLOCKS)
ORDER = GATHERED + PICKED
TURNED = 1 + len(GATHERED)

TILE = 128
CHUNK = 256
TILES = CHUNK // TILE
CHUNKS = BATCH // CHUNK
QUAD = 4
QUADS = TURNED // QUAD
GROUP = 4
G = F - 1
GF, GG = GROUP * F, GROUP * G
GROUPS = TILE // GROUP
UNIT = 4
UNITS = GROUPS // UNIT
GRAM_BANKS = 3
EARLY = 2
LENT = max(u for u in range(UNITS) if u % GRAM_BANKS == 2)
HALVES = ((0, 0), (0, 1), (1, 0))
BANK = 512
NPICK = len(PICKED)
PAIRS_PICKED = -(-NPICK // 2)
STAGED = 4
HOTS = 3

HALF = F // 2
RUNS = [(d - 1, G, G + 1) for d in range(1, HALF + 1)] + [(G - HALF, HALF, 1)]
PAIRS = sum(n for _, n, _ in RUNS)
KP = 117
KSTEPS = PAIRS // KP

assert HOTS == 3 and QUADS == 5 and H2 == 2 * P and UNITS >= 2 * KSTEPS
assert TURNED % QUAD == 0 and GROUPS % UNIT == 0 and UNITS % GRAM_BANKS == 2 and PAIRS_PICKED % 2 == 0
assert NPICK == STAGED + 3
assert KSTEPS == 3 and H1 == 4 * P
assert PAIRS == KP * KSTEPS and all(VOCAB[f] % RP == 0 for f in PICKED)


def pair_runs():
    out, row = [], 0
    for q, n, step in RUNS:
        while n:
            take = min(n, KP - row % KP)
            out.append((q, take, step, row // KP, row % KP))
            q, n, row = q + step * take, n - take, row + take
    return out


def pair_rows():
    index = {}
    for a in range(F):
        for b in range(a + 1, F):
            index[(a, b)] = D + len(index)
    feature = [0] + [f + 1 for f in ORDER]
    rows = []
    for q, n, step, _, _ in pair_runs():
        for entry in range(q, q + step * n, step):
            a, b = divmod(entry, G)
            rows.append(index[tuple(sorted((feature[a], feature[b + 1])))])
    assert sorted(rows) == sorted(index.values())
    return rows


def build(nc, dense, ids, ids_t, tables, w_pairs, w_dense, b1, w2, b2, w3, y_out):
    with ExitStack() as ctx:
        def sb(name, shape, dt=F32):
            return ctx.enter_context(nc.sbuf_tensor(name, shape, dt))

        def psum(name, shape):
            return ctx.enter_context(nc.psum_tensor(name, shape, F32))

        def sem(name):
            return ctx.enter_context(nc.semaphore(name))

        gram_dram = nc.dram_tensor("gram_scratch", (TILES, GROUP, F, G, GROUPS), F32, kind="Internal").ap()

        ident = sb("ident", [P, P])
        ids_sb = [sb(f"ids{t}", [P, TABLES], I32) for t in range(TILES)]
        rows_sb = [sb(f"rows{t}", [P, TURNED, D]) for t in range(TILES)]
        feat_sb = [sb(f"feat{t}", [P, GROUPS, GROUP, F]) for t in range(TILES)]
        gram_sb = [sb(f"gram{t}", [P, GG, GROUPS]) for t in range(TILES)]
        table_sb = [sb(f"table{i}", [RP, 2, BLOCKS[i], D], F32R) for i in range(NPICK)]
        picks_sb = sb("picks", [RP, NPICK, CHUNK], I32)
        row_id = {n: sb(f"row_id{n}", [P, n], I32) for n in sorted(set(BLOCKS))}
        hot_sb = [sb(f"hot{i}", [RP, max(BLOCKS[i::HOTS]), CHUNK], F32R) for i in range(HOTS)]
        pairs_raw = sb("pairs_raw", [KP, KSTEPS, CHUNK])
        pairs_sb = sb("pairs", [KP, 2, KSTEPS, CHUNK], F32R)
        dense_sb = sb("dense_t", [P, 2, CHUNK], F32R)
        h1_sb = sb("h1", [P, H1 // P, CHUNK])
        h2_sb = sb("h2", [P, H2 // P, CHUNK])
        y_sb = sb("y", [P, BATCH // TILE - 1])
        y_rows = sb("y_rows", [BATCH // TILE - 1, TILE])
        y_last = sb("y_last", [1, TILE])
        w_pairs_sb = sb("w_pairs_sb", [KP, 2, KSTEPS, H1], F32R)
        w_pairs_stage = gram_sb[1].rearrange("p q n -> p (q n)")[
            0:KP, MAX_BLOCKS * D:MAX_BLOCKS * D + KSTEPS * H1].rearrange("p (k n) -> p k n", k=KSTEPS)
        w_dense_stage = h1_sb.rearrange("p k n -> p (k n)").rearrange("p (k n) -> p k n", k=2)
        last = rows_sb[0].rearrange("p f d -> p (f d)")
        w_pairs_last = last[0:KP, 0:KSTEPS * H1].rearrange("p (k n) -> p k n", k=KSTEPS)
        w_dsum_last = last[:, KSTEPS * H1:(KSTEPS + 1) * H1]
        dense_last = last[:, (KSTEPS + 1) * H1:(KSTEPS + 1) * H1 + CHUNK]
        w_dsum_sb = sb("w_dsum_sb", [P, 2, H1], F32R)
        w2_sb = sb("w2_sb", [P, H1 // P, H2])
        w3_sb = sb("w3_sb", [P, H2 // P])
        b1_sb = sb("b1_sb", [P, H1 // P])
        b2_sb = sb("b2_sb", [P, H2 // P])

        turn_ps = [psum(f"turn{i}", [P, QUAD, TILE]) for i in range(2)]
        pick_ps = [psum(f"pickps{i}", [P, 2, CHUNK]) for i in range(2)]
        gram_ps = [psum(f"gramps{i}", [P, BANK]) for i in range(2)] + [pick_ps[0].rearrange("p i n -> p (i n)")]
        top_ps = [psum(f"top{i}", [P, BANK]) for i in range(2)]
        last_ps = top_ps + gram_ps[0:2]
        y_ps = pick_ps[1].rearrange("p i n -> p (i n)")

        weights_in = sem("weights_in")
        ident_zero = sem("ident_zero")
        ident_ready = sem("ident_ready")
        staged = [sem(f"staged{i}") for i in range(STAGED)]
        split_high = sem("split_high")
        split_low = sem("split_low")
        ids_in = [sem(f"ids_in{t}") for t in range(TILES)]
        picks_in = sem("picks_in")
        dense_in = [sem(f"dense_in{t}") for t in range(TILES)]
        gathered = [[sem(f"gathered{t}_{q}") for q in range(QUADS)] for t in range(TILES)]
        turned = sem("turned")
        feat_act = sem("feat_act")
        feat_dve = sem("feat_dve")
        hot_made = sem("hot_made")
        picked = sem("picked")
        pick_out = sem("pick_out")
        gram_made = sem("gram_made")
        gram_out = sem("gram_out")
        scratch_in = [sem(f"scratch_in{t}") for t in range(TILES)]
        pairs_in = sem("pairs_in")
        pairs_last = [sem(f"pairs_last{k}") for k in range(KSTEPS)]
        pairs_high = sem("pairs_high")
        pairs_low = sem("pairs_low")
        w_high = sem("w_high")
        w_low = sem("w_low")
        w_last_in = sem("w_last_in")
        last_made = sem("last_made")
        w_summed = sem("w_summed")
        dense_high = sem("dense_high")
        dense_copied = sem("dense_copied")
        top1_made = sem("top1_made")
        h1_ready = sem("h1_ready")
        top2_made = sem("top2_made")
        h2_ready = sem("h2_ready")
        top3_made = sem("top3_made")
        y_free = sem("y_free")
        y_turned = sem("y_turned")
        y_ready = sem("y_ready")
        y_written = sem("y_written")

        NB1, NB2 = H1 // P, H2 // P
        WEIGHTS = 6
        ACT_QUADS, DVE_QUADS = (QUADS + 1) // 2, QUADS // 2
        runs = pair_runs()
        runs_of_step = [[run for run in runs if run[3] == k] for k in range(KSTEPS)]
        CALL_A, CALL_B = CHUNKS - 1, CHUNKS

        def columns(call):
            if isinstance(call, int) and call >= CALL_A:
                return slice(TILE * (call - CALL_A), TILE * (call - CALL_A + 1)), TILE
            return slice(0, CHUNK), CHUNK

        def run_of_tile(t, q, n, step, k, row):
            flat = gram_dram[t].rearrange("s f g n -> (f g) s n")
            return (pairs_raw[row:row + n, k, TILE * t:TILE * t + TILE].rearrange("p (s n) -> p s n", n=GROUPS),
                    flat[q:q + step * (n - 1) + 1:step])

        def slots_of(q):
            return [f for f in range(QUAD * q, QUAD * q + QUAD) if f > 0]

        def started(c):
            return not isinstance(c, int) or c > 0

        def feat_out(t, q):
            return feat_sb[t][:, :, :, QUAD * q:QUAD * q + QUAD].rearrange("p n s f -> p f s n")

        def feat_in(q):
            return turn_ps[q % 2][:].rearrange("p f (s n) -> p f s n", s=GROUP)

        def last_user(i):
            return max(k for k in range(NPICK) if k % HOTS == i % HOTS)

        def stage(i, n):
            flat = gram_sb[i % STAGED // 2].rearrange("p q n -> p (q n)")
            at = i % 2 * MAX_BLOCKS * D
            return flat[0:RP, at:at + n * D].rearrange("p (j d) -> p j d", d=D)

        block = ctx.enter_context(nc.Block())

        @block.sync
        def _(sp):
            def load_ids(t, c):
                sp.dma_start(ids_sb[t][:], ids[bass.ds(c * CHUNK + t * TILE, TILE), :]).then_inc(ids_in[t], 16)

            def load_dense(t, c):
                sp.dma_start(rows_sb[t][:, 0, :],
                             dense[bass.ds(c * CHUNK + t * TILE, TILE), :]).then_inc(dense_in[t], 16)

            def load_picks(c):
                sp.dma_start(picks_sb[:], ids_t[:, bass.ds(c * CHUNK, CHUNK)].unsqueeze(0)
                             .to_broadcast([RP, NPICK, CHUNK])).then_inc(picks_in, 16)

            def load_table(i):
                sp.dma_start(stage(i, BLOCKS[i]), tables[PICKED[i]].rearrange("(p j) d -> p j d", p=RP)
                             ).then_inc(staged[i % STAGED], 16)

            def next_tile(t, c):
                landed = sp.to_reg(16 * QUAD * c) if started(c - 1) else 16 * QUAD
                landed0 = sp.to_reg(16 * (QUAD - 1) * c) if started(c - 1) else 16 * (QUAD - 1)
                sp.wait_ge(ids_in[t], 16)
                for q in range(1, QUADS):
                    sp.wait_ge(gathered[t][q], landed)
                sp.wait_ge(gathered[t][0], landed0)
                load_ids(t, c)
                freed = QUADS * (TILES * (c - 1) + t) + 1
                if started(c - 1):
                    freed = sp.to_reg(freed)
                sp.wait_ge(dense_in[t], 16)
                sp.wait_ge(turned, freed)
                load_dense(t, c)

            def next_picks(c):
                made = NPICK * c if isinstance(c, int) else sp.to_reg(NPICK * c)
                sp.wait_ge(picks_in, 16)
                sp.wait_ge(hot_made, made)
                load_picks(c)

            def write_gram(t, c):
                sp.wait_ge(gram_out, UNITS * (TILES * c + t + 1))
                for s in range(GROUP):
                    sp.dma_start(gram_dram[t, s].rearrange("f g n -> f (g n)"),
                                 gram_sb[t][F * s:F * s + F, G * s:G * s + G, :]
                                 .rearrange("p g n -> p (g n)")).then_inc(scratch_in[t], 16)

            def read_pairs(c):
                for t in range(TILES):
                    sp.wait_ge(scratch_in[t], 16 * GROUP)
                    sp.wait_ge(scratch_in[t], 16 * GROUP * (c + 1))
                if started(c):
                    split = KSTEPS * c if isinstance(c, int) else sp.to_reg(KSTEPS * c)
                    sp.wait_ge(pairs_low, split)
                flat = gram_dram.rearrange("t s f g n -> (f g) (t s) n")
                for q, n, step, k, row in runs:
                    sp.dma_start(pairs_raw[row:row + n, k, :].rearrange("p (u n) -> p u n", n=GROUPS),
                                 flat[q:q + step * (n - 1) + 1:step]).then_inc(pairs_in, 16)

            def chunk(c, last):
                read = 16 * len(runs) * c if isinstance(c, int) else sp.to_reg(16 * len(runs) * c)
                if not last:
                    next_tile(0, c + 1)
                    next_picks(c + 1)
                sp.wait_ge(scratch_in[0], 16)
                sp.wait_ge(pairs_in, read)
                write_gram(0, c)
                if not last:
                    next_tile(1, c + 1)
                    write_gram(1, c)
                    read_pairs(c)

            def read_tile_pairs(t, done):
                sp.wait_ge(pairs_low, KSTEPS * (CHUNKS - 1))
                sp.wait_ge(scratch_in[t], 16 * GROUP * CHUNKS)
                for q, n, step, k, row in (runs if t < TILES - 1 else runs_of_step[0] + runs_of_step[1]):
                    sp.dma_start(*run_of_tile(t, q, n, step, k, row)).then_inc(done[k], 16)

            load_ids(0, 0)
            load_picks(0)
            load_table(0)
            load_table(1)
            load_ids(1, 0)
            load_table(2)
            load_table(3)
            load_dense(0, 0)
            for i in range(STAGED, NPICK):
                sp.wait_ge(split_low, i - STAGED + 1)
                load_table(i)
            load_dense(1, 0)
            sp.wait_ge(split_low, STAGED)
            sp.dma_start(w_pairs_stage, w_pairs.rearrange("(k p) n -> p k n", p=KP)).then_inc(weights_in, 16)
            sp.dma_start(w_dense_stage, w_dense.rearrange("(k p) n -> p k n", p=P)).then_inc(weights_in, 16)
            sp.dma_start(w2_sb[:], w2.rearrange("(k p) n -> p k n", p=P)).then_inc(weights_in, 16)
            sp.dma_start(w3_sb[:], w3).then_inc(weights_in, 16)
            sp.dma_start(b1_sb[:], b1).then_inc(weights_in, 16)
            sp.dma_start(b2_sb[:], b2).then_inc(weights_in, 16)
            next_picks(1)
            next_tile(0, 1)
            write_gram(0, 0)
            next_tile(1, 1)
            write_gram(1, 0)
            read_pairs(0)
            with sp.Fori(1, CHUNKS - 1) as c:
                chunk(c, False)
            chunk(CHUNKS - 1, True)
            sp.wait_ge(turned, QUADS * (TILES * (CHUNKS - 1) + 1))
            sp.dma_start(w_pairs_last, w_pairs.rearrange("(k p) n -> p k n", p=KP)).then_inc(w_last_in, 16)
            read_tile_pairs(0, [pairs_in] * KSTEPS)
            write_gram(1, CHUNKS - 1)
            read_tile_pairs(1, pairs_last)
            sp.wait_ge(y_ready, 1)
            sp.dma_start(y_out[0:BATCH // TILE - 1, :], y_rows[:]).then_inc(y_written, 16)
            sp.wait_ge(y_free, 1 + CHUNKS + 1)
            sp.dma_start(y_out[BATCH // TILE - 1:BATCH // TILE, :], y_last[:]).then_inc(y_written, 16)
            sp.wait_ge(y_written, 32)

        @block.gpsimd
        def _(pool):
            def chunk(c):
                for t in range(TILES):
                    pool.wait_ge(ids_in[t], 16 * (c + 1))
                    for q in range(QUADS):
                        if started(c):
                            freed = pool.to_reg(QUADS * (TILES * (c - 1) + t) + q + 1)
                            pool.wait_ge(ids_in[t], 16)
                            pool.wait_ge(turned, freed)
                        for f in slots_of(q):
                            table = ORDER[f - 1]
                            nc.gpsimd.indirect_dma_start(
                                out=rows_sb[t][:, f, :], out_offset=None, in_=tables[table][:, :],
                                in_offset=bass.IndirectOffsetOnAxis(ap=ids_sb[t][:, table:table + 1], axis=0),
                            ).then_inc(gathered[t][q], 16)

            for n in row_id:
                nc.gpsimd.iota(row_id[n][:], pattern=[[1, n]], base=0, channel_multiplier=n).then_inc(ident_ready, 1)
            nc.gpsimd.memset(ident[:], 0.0).then_inc(ident_zero, 1)
            pool.wait_ge(ident_zero, 1)
            nc.gpsimd.affine_select(out=ident[:], in_=ident[:], compare_op=ALU.not_equal, fill=1.0, base=0,
                                    pattern=[[-1, P]], channel_multiplier=1).then_inc(ident_ready, 1)
            chunk(0)
            with pool.Fori(1, CHUNKS) as c:
                chunk(c)
            pool.wait_ge(pairs_low, KSTEPS * (CHUNKS - 1))
            pool.wait_ge(scratch_in[1], 16 * GROUP * CHUNKS)
            for run in runs_of_step[2]:
                nc.gpsimd.dma_start(*run_of_tile(1, *run)).then_inc(pairs_last[2], 16)

        @block.tensor
        def _(pe):
            def transposes(t, c, q):
                tile = TILES * c + t
                if q == 0:
                    pe.wait_ge(dense_in[t], 16 * (c + 1))
                pe.wait_ge(gathered[t][q], 16 * len(slots_of(q)) * (c + 1))
                before = (ACT_QUADS if q % 2 == 0 else DVE_QUADS) * tile + q // 2
                if not isinstance(before, int) or before > 0:
                    pe.wait_ge(feat_act if q % 2 == 0 else feat_dve, before)
                for j in range(QUAD):
                    last = nc.tensor.transpose(turn_ps[q % 2][:, j, :], rows_sb[t][:, QUAD * q + j, :], ident[:])
                last.then_inc(turned, 1)

            def pick(i, c):
                pe.wait_ge(hot_made, NPICK * c + i + 1)
                if not started(c):
                    pe.wait_ge(split_low, i + 1)
                before = PAIRS_PICKED * c + i // 2 - 1
                if i % 2 == 0 and (started(c) or before > 0):
                    pe.wait_ge(pick_out, before)
                if i == 0 and started(c):
                    pe.wait_ge(gram_out, UNITS * (TILES * c - 1) + LENT + 1)
                for j in range(BLOCKS[i]):
                    for half in range(2):
                        last = nc.tensor.matmul(pick_ps[i // 2 % 2][:, i % 2, :], table_sb[i][:, half, j, :],
                                                hot_sb[i % HOTS][:, j, :], start=(j == 0 and half == 0),
                                                stop=(j == BLOCKS[i] - 1 and half == 1))
                last.then_inc(picked, 1)

            def gram(t, c, u):
                tile = TILES * c + t
                if u == 0:
                    pe.wait_ge(feat_act, ACT_QUADS * (tile + 1))
                    pe.wait_ge(feat_dve, DVE_QUADS * (tile + 1))
                    pe.wait_ge(pick_out, PAIRS_PICKED * (c + 1))
                before = UNITS * tile + (u - GRAM_BANKS + 1 if u >= GRAM_BANKS else u - 1)
                if u >= GRAM_BANKS or (u < 2 and (not isinstance(before, int) or before > 0)):
                    pe.wait_ge(gram_out, before)
                for j in range(UNIT):
                    x = feat_sb[t][:, UNIT * u + j]
                    last = nc.tensor.matmul(
                        gram_ps[u % GRAM_BANKS][0:GF, GG * j:GG * j + GG].rearrange("p (s g) -> p s g", g=G),
                        x.rearrange("p s f -> p (s f)"), x[:, :, 1:F], start=True, stop=True)
                last.then_inc(gram_made, 1)

            def layer1(call, m):
                cols, n = columns(call)
                tail = n < CHUNK
                if m == 0:
                    if not tail:
                        pe.wait_ge(pairs_low, KSTEPS * (call + 1))
                        pe.wait_ge(dense_copied, TILES * (call + 1))
                    else:
                        pe.wait_ge(w_last_in, 16)
                        pe.wait_ge(pairs_in, 16 * len(runs) * CHUNKS)
                        pe.wait_ge(last_made, 1 + TILES)
                if tail and m < 2:
                    pe.wait_ge(h2_ready, NB2 * (call - 1) + m + 1)
                if m >= 2:
                    pe.wait_ge(h1_ready, NB1 * call + m - 1)
                ps = top_ps[m % 2][:, 0:n]
                for k in range(KSTEPS):
                    if tail:
                        nc.tensor.matmul(ps, w_pairs_last[:, k, P * m:P * m + P], pairs_raw[:, k, cols],
                                         start=(k == 0), stop=False)
                        continue
                    for w_half, x_half in HALVES:
                        nc.tensor.matmul(ps, w_pairs_sb[:, w_half, k, P * m:P * m + P],
                                         pairs_sb[:, x_half, k, :],
                                         start=(k == 0 and w_half == x_half), stop=False)
                if tail:
                    done = nc.tensor.matmul(ps, w_dsum_last[:, P * m:P * m + P], dense_last[:, cols],
                                            start=False, stop=True)
                else:
                    for w_half, x_half in HALVES:
                        done = nc.tensor.matmul(ps, w_dsum_sb[:, w_half, P * m:P * m + P], dense_sb[:, x_half, :],
                                                start=False, stop=(w_half, x_half) == HALVES[-1])
                done.then_inc(top1_made, 1)

            def layer1_last(k):
                cols, n = columns(CALL_B)
                if k >= 0:
                    pe.wait_ge(pairs_last[k], 16 * len(runs_of_step[k]))
                for m in range(NB1):
                    if k < 0 and m < 2:
                        pe.wait_ge(h2_ready, NB2 * CALL_A + m + 1)
                    elif k < 0:
                        pe.wait_ge(gram_out, UNITS * TILES * CHUNKS)
                    w = w_dsum_last if k < 0 else w_pairs_last[:, k, :]
                    x = dense_last if k < 0 else pairs_raw[:, k, :]
                    done = nc.tensor.matmul(last_ps[m][:, 0:n], w[:, P * m:P * m + P], x[:, cols],
                                            start=(k < 0), stop=(k == KSTEPS - 1))
                    if k == KSTEPS - 1:
                        done.then_inc(top1_made, 1)

            def layer2(call, m):
                cols, n = columns(call)
                ps = top_ps[m % 2][:, 0:n]
                for k in range(NB1):
                    if m == 0:
                        own_banks = isinstance(call, int) and call == CALL_B
                        pe.wait_ge(h1_ready, NB1 * call + (k if own_banks else max(k, 2)) + 1)
                    elif k == 0:
                        pe.wait_ge(h1_ready, NB1 * (call + 1))
                    last = nc.tensor.matmul(ps, w2_sb[:, k, P * m:P * m + P], h1_sb[:, k, cols],
                                            start=(k == 0), stop=(k == NB1 - 1))
                last.then_inc(top2_made, 1)

            def layer3(call):
                cols, n = columns(call)
                pe.wait_ge(h2_ready, NB2 * (call + 1))
                pe.wait_ge(y_free, call + 1)
                for t in range(n // TILE):
                    at = cols.start + TILE * t
                    for k in range(NB2):
                        last = nc.tensor.matmul(y_ps[:, t:t + 1], h2_sb[:, k, at:at + TILE],
                                                w3_sb[:, k:k + 1], start=(k == 0), stop=(k == NB2 - 1))
                last.then_inc(top3_made, 1)

            def layer3_last():
                cols, n = columns(CALL_B)
                pe.wait_ge(h2_ready, NB2 * (CALL_B + 1))
                for k in range(NB2):
                    last = nc.tensor.matmul(y_ps[0:1, 0:n], w3_sb[:, k:k + 1], h2_sb[:, k, cols],
                                            start=(k == 0), stop=(k == NB2 - 1))
                last.then_inc(top3_made, 1)

            def picks(c):
                for i in range(NPICK):
                    pick(i, c)
                    if i > 0 and i <= QUADS:
                        transposes(0, c, i - 1)

            pe.wait_ge(ident_ready, 1 + len(row_id))
            picks(0)
            for u in range(UNITS):
                gram(0, 0, u)
            for q in range(QUADS):
                transposes(1, 0, q)
            for u in range(EARLY):
                gram(1, 0, u)
            pe.wait_ge(weights_in, 16 * WEIGHTS)
            pe.wait_ge(w_low, 1)
            pe.wait_ge(y_free, 1)
            with pe.Fori(1, CHUNKS - 1) as c:
                for u in range(EARLY, UNITS):
                    gram(1, c - 1, u)
                picks(c)
                transposes(1, c, 0)
                for u in range(UNITS):
                    gram(0, c, u)
                for m in range(NB1):
                    layer1(c - 1, m)
                transposes(1, c, 1)
                transposes(1, c, 2)
                layer2(c - 1, 0)
                transposes(1, c, 3)
                transposes(1, c, 4)
                layer2(c - 1, 1)
                for u in range(EARLY):
                    gram(1, c, u)
                layer3(c - 1)
            c = CHUNKS - 1
            for u in range(EARLY, UNITS):
                gram(1, c - 1, u)
            picks(c)
            for u in range(UNITS):
                gram(0, c, u)
            for m in range(NB1):
                layer1(c - 1, m)
            transposes(1, c, 0)
            transposes(1, c, 1)
            layer2(c - 1, 0)
            for q in range(2, QUADS):
                transposes(1, c, q)
            for u in range(UNITS):
                gram(1, c, u)
            layer2(c - 1, 1)
            layer1(CALL_A, 0)
            layer3(CHUNKS - 2)
            for m in range(1, NB1):
                layer1(CALL_A, m)
            layer2(CALL_A, 0)
            layer2(CALL_A, 1)
            layer1_last(-1)
            layer3(CALL_A)
            layer1_last(0)
            pe.wait_ge(y_free, 1 + CHUNKS)
            nc.tensor.transpose(pick_ps[0][0:BATCH // TILE - 1, 0, 0:TILE], y_sb[:], ident[:]).then_inc(y_turned, 1)
            layer1_last(1)
            layer1_last(2)
            layer2(CALL_B, 0)
            layer2(CALL_B, 1)
            layer3_last()

        @block.scalar
        def _(act):
            def copy_quad(t, c, q):
                tile = TILES * c + t
                if q == 0 and started(c):
                    act.wait_ge(dense_copied, TILES * (c - 1) + t + 1)
                act.wait_ge(turned, QUADS * tile + q + 1)
                nc.scalar.copy(feat_out(t, q), feat_in(q)).then_inc(feat_act, 1)

            def copy_picked(k, c):
                n = min(2, NPICK - 2 * k)
                act.wait_ge(picked, NPICK * c + min(2 * k + 2, NPICK))
                for t in range(TILES):
                    at = TURNED + 2 * k
                    last = nc.scalar.copy(
                        feat_sb[t][:, :, :, at:at + n].rearrange("p n s f -> p f s n"),
                        pick_ps[k % 2][:, 0:n, TILE * t:TILE * t + TILE].rearrange("p f (s n) -> p f s n", s=GROUP))
                last.then_inc(pick_out, 1)

            def copy_gram(t, c, u):
                if u == 0 and started(c):
                    act.wait_ge(scratch_in[t], 16 * GROUP * c)
                if u == 0 and not started(c):
                    act.wait_ge(split_low, NPICK)
                    if t == 1:
                        act.wait_ge(w_low, 1)
                act.wait_ge(gram_made, UNITS * (TILES * c + t) + u + 1)
                nc.scalar.copy(gram_sb[t][0:GF, :, UNIT * u:UNIT * u + UNIT].rearrange("p q n -> p n q"),
                               gram_ps[u % GRAM_BANKS][0:GF, 0:UNIT * GG].rearrange("p (n q) -> p n q", q=GG)
                               ).then_inc(gram_out, 1)

            def layer1(call, m):
                cols, n = columns(call)
                act.wait_ge(top1_made, NB1 * call + m + 1)
                last = isinstance(call, int) and call == CALL_B
                nc.scalar.activation(h1_sb[:, m, cols], (last_ps[m] if last else top_ps[m % 2])[:, 0:n], ACT.Relu,
                                     bias=b1_sb[:, m:m + 1]).then_inc(h1_ready, 1)

            def split_pairs(c, k):
                if k == 0:
                    act.wait_ge(pairs_in, 16 * len(runs) * (c + 1))
                nc.scalar.copy(pairs_sb[:, 0, k, :], pairs_raw[:, k, :]).then_inc(pairs_high, 1)

            def gram_a_and_split(c):
                for u in range(UNITS):
                    copy_gram(0, c, u)
                    if u % 2 == 1 and u < 2 * KSTEPS:
                        split_pairs(c - 1, u // 2)

            def copies_of_picks(c):
                for i in range(NPICK):
                    if i % 2 == 1 or i == NPICK - 1:
                        copy_picked(i // 2, c)
                    if i > 0 and i <= QUADS and i % 2 == 1:
                        copy_quad(0, c, i - 1)

            for i in range(NPICK):
                act.wait_ge(staged[i % STAGED], 16 * (i // STAGED + 1))
                nc.scalar.copy(table_sb[i][:, 0], stage(i, BLOCKS[i])).then_inc(split_high, 1)
            copies_of_picks(0)
            act.wait_ge(weights_in, 16 * WEIGHTS)
            nc.scalar.copy(w_pairs_sb[:, 0], w_pairs_stage).then_inc(w_high, 1)
            act.wait_ge(w_summed, 1)
            nc.scalar.copy(w_dsum_sb[:, 0], w_dense_stage[:, 0, :]).then_inc(w_high, 1)
            for u in range(UNITS):
                copy_gram(0, 0, u)
            for q in range(0, QUADS, 2):
                copy_quad(1, 0, q)
            with act.Fori(1, CHUNKS - 1) as c:
                for u in range(UNITS):
                    copy_gram(1, c - 1, u)
                copies_of_picks(c)
                copy_quad(1, c, 0)
                gram_a_and_split(c)
                for m in range(NB1):
                    layer1(c - 1, m)
                copy_quad(1, c, 2)
                copy_quad(1, c, 4)
            c = CHUNKS - 1
            for u in range(UNITS):
                copy_gram(1, c - 1, u)
            copies_of_picks(c)
            gram_a_and_split(c)
            for m in range(NB1):
                layer1(c - 1, m)
            for q in range(0, QUADS, 2):
                copy_quad(1, c, q)
            for u in range(UNITS):
                copy_gram(1, c, u)
            for call in (CALL_A, CALL_B):
                for m in range(NB1):
                    layer1(call, m)

        @block.vector
        def _(dve):
            def one_hot(i, c):
                if i == 0:
                    dve.wait_ge(picks_in, 16 * (c + 1))
                before = NPICK * (c - 1) + last_user(i) + 1 if i < HOTS else NPICK * c + i - HOTS + 1
                if started(c) or i >= HOTS:
                    dve.wait_ge(picked, before)
                for j in range(BLOCKS[i]):
                    last = nc.vector.tensor_scalar(hot_sb[i % HOTS][:, j, :], picks_sb[:, i, :],
                                                   row_id[BLOCKS[i]][0:RP, j:j + 1], None, ALU.is_equal)
                last.then_inc(hot_made, 1)

            def copy_quad(t, c, q):
                dve.wait_ge(turned, QUADS * (TILES * c + t) + q + 1)
                nc.vector.tensor_copy(feat_out(t, q), feat_in(q)).then_inc(feat_dve, 1)

            def by_sample(x, t):
                return x[:, TILE * t:TILE * t + TILE].rearrange("p (s n) -> p s n", s=GROUP)

            def dense_copies(c):
                dve.wait_ge(feat_act, ACT_QUADS * (TILES * c + 1) + 1)
                for t in range(TILES):
                    nc.vector.tensor_copy(by_sample(dense_sb[:, 0], t), feat_sb[t][:, :, :, 0].rearrange(
                        "p n s -> p s n")).then_inc(dense_high, 1)
                for t in range(TILES):
                    dve.wait_ge(dense_high, TILES * c + t + 1)
                    nc.vector.tensor_tensor(
                        by_sample(dense_sb[:, 1], t), feat_sb[t][:, :, :, 0].rearrange("p n s -> p s n"),
                        by_sample(dense_sb[:, 0], t), ALU.subtract).then_inc(dense_copied, 1)

            def last_copies(c):
                dve.wait_ge(turned, QUADS * (TILES * c + 1))
                nc.vector.tensor_tensor(w_dsum_last, w_dsum_sb[:, 0], w_dsum_sb[:, 1], ALU.add).then_inc(last_made, 1)
                dve.wait_ge(feat_act, ACT_QUADS * (TILES * c + 1) + 1)
                for t in range(TILES):
                    nc.vector.tensor_copy(by_sample(dense_last, t), feat_sb[t][:, :, :, 0].rearrange(
                        "p n s -> p s n")).then_inc(last_made, 1)

            def layer2(call, m):
                cols, n = columns(call)
                dve.wait_ge(top2_made, NB2 * call + m + 1)
                nc.vector.tensor_scalar(h2_sb[:, m, cols], top_ps[m % 2][:, 0:n], b2_sb[:, m:m + 1], 0.0,
                                        ALU.add, ALU.max).then_inc(h2_ready, 1)

            def layer3(call):
                cols, n = columns(call)
                at = (CHUNKS - 1) * TILES + cols.start // TILE if n < CHUNK else call * TILES
                dve.wait_ge(top3_made, call + 1)
                nc.vector.tensor_copy(y_sb[:, bass.ds(at, n // TILE)],
                                      y_ps[:, 0:n // TILE]).then_inc(y_free, 1)

            def split_pairs(c):
                for k in range(KSTEPS):
                    dve.wait_ge(pairs_high, KSTEPS * c + k + 1)
                    nc.vector.tensor_tensor(pairs_sb[:, 1, k, :], pairs_raw[:, k, :], pairs_sb[:, 0, k, :],
                                            ALU.subtract).then_inc(pairs_low, 1)

            def picks(c):
                for i in range(HOTS, NPICK):
                    one_hot(i, c)
                    if i % 2 == 0:
                        copy_quad(0, c, i - HOTS)

            dve.wait_ge(ident_ready, 1 + len(row_id))
            for i in range(NPICK):
                dve.wait_ge(split_high, i + 1)
                nc.vector.tensor_tensor(table_sb[i][:, 1], stage(i, BLOCKS[i]), table_sb[i][:, 0],
                                        ALU.subtract).then_inc(split_low, 1)
                one_hot(i, 0)
                if i == 5:
                    copy_quad(0, 0, 1)
            copy_quad(0, 0, 3)
            dve.wait_ge(weights_in, 16 * WEIGHTS)
            nc.vector.tensor_tensor(w_dense_stage[:, 0, :], w_dense_stage[:, 0, :], w_dense_stage[:, 1, :],
                                    ALU.add).then_inc(w_summed, 1)
            dve.wait_ge(w_high, 1)
            nc.vector.tensor_tensor(w_pairs_sb[:, 1], w_pairs_stage, w_pairs_sb[:, 0],
                                    ALU.subtract).then_inc(w_low, 1)
            dve.wait_ge(w_high, 2)
            nc.vector.tensor_tensor(w_dsum_sb[:, 1], w_dense_stage[:, 0, :], w_dsum_sb[:, 0],
                                    ALU.subtract).then_inc(y_free, 1)
            one_hot(0, 1)
            one_hot(1, 1)
            copy_quad(1, 0, 1)
            copy_quad(1, 0, 3)
            dense_copies(0)
            one_hot(2, 1)
            with dve.Fori(1, CHUNKS - 1) as c:
                picks(c)
                split_pairs(c - 1)
                copy_quad(1, c, 1)
                layer2(c - 1, 0)
                copy_quad(1, c, 3)
                layer2(c - 1, 1)
                dense_copies(c)
                one_hot(0, c + 1)
                layer3(c - 1)
                for i in range(1, HOTS):
                    one_hot(i, c + 1)
            c = CHUNKS - 1
            picks(c)
            split_pairs(c - 1)
            copy_quad(1, c, 1)
            copy_quad(1, c, 3)
            last_copies(c)
            layer2(c - 1, 0)
            layer2(c - 1, 1)
            layer3(c - 1)
            layer2(CALL_A, 0)
            layer2(CALL_A, 1)
            layer3(CALL_A)
            dve.wait_ge(y_turned, 1)
            nc.vector.tensor_copy(y_rows[:], pick_ps[0][0:BATCH // TILE - 1, 0, 0:TILE]).then_inc(y_ready, 1)
            layer2(CALL_B, 0)
            layer2(CALL_B, 1)
            dve.wait_ge(top3_made, CALL_B + 1)
            nc.vector.tensor_copy(y_last[:], y_ps[0:1, 0:TILE]).then_inc(y_free, 1)


def kernel(**inputs):
    import concourse.bacc as bacc
    from concourse.bass_utils import run_bass_kernel_spmd

    def column_blocks(a):
        return np.ascontiguousarray(np.asarray(a).reshape(-1, P).T)

    w1 = np.asarray(inputs["W_top1"])
    ids = np.ascontiguousarray(inputs["ids"])
    arrays = {
        "dense": np.ascontiguousarray(inputs["r_dense_output"]),
        "ids": ids,
        "ids_t": np.ascontiguousarray(ids.T[PICKED]),
        "w_pairs": np.ascontiguousarray(w1[np.array(pair_rows())]),
        "w_dense": np.concatenate([w1[:D], w1[D + PAIRS:]]),
        "b1": column_blocks(inputs["b_top1"]),
        "w2": np.ascontiguousarray(inputs["W_top2"]),
        "b2": column_blocks(inputs["b_top2"]),
        "w3": column_blocks(inputs["W_top3"]),
    }
    for f in range(TABLES):
        arrays[f"tbl_{f}"] = np.ascontiguousarray(inputs[f"tbl_{f}"])
    nc = bacc.Bacc("TRN2", target_bir_lowering=False, num_devices=1)
    ap = {n: nc.dram_tensor(n, a.shape, mybir.dt.from_np(a.dtype), kind="ExternalInput").ap()
          for n, a in arrays.items()}
    y = nc.dram_tensor("y_out", (BATCH // TILE, TILE), F32, kind="ExternalOutput").ap()
    build(nc, ap["dense"], ap["ids"], ap["ids_t"], [ap[f"tbl_{f}"] for f in range(TABLES)], ap["w_pairs"],
          ap["w_dense"], ap["b1"], ap["w2"], ap["b2"], ap["w3"], y)
    result = run_bass_kernel_spmd(nc, [arrays], core_ids=[0])
    return result.results[0]["y_out"].reshape(BATCH, 1)
```
